# Optimizing a Trainium2 kernel written in Bass

```python
import numpy as np
import jax
import jax.numpy as jnp

def _softmax(x, axis=-1):
    return jax.nn.softmax(x, axis=axis)

def _gelu(x):
    return jax.nn.gelu(x, approximate=True)

def _silu(x):
    return jax.nn.silu(x)

def _sigmoid(x):
    return jax.nn.sigmoid(x)

def _layernorm(x, axis=-1, eps=1e-05):
    m = jnp.mean(x, axis=axis, keepdims=True)
    v = jnp.var(x, axis=axis, keepdims=True)
    return (x - m) / jnp.sqrt(v + eps)

def _scatter_add(tgt, idx, src, axis=0):
    return tgt.at[idx].add(src)

def _segment_sum(src, seg, n):
    return jax.ops.segment_sum(src, seg, n)
kernel_name = 'mk_dlrm_tower_d1_rec_r8_2b502e'

def setup_inputs(seed: int=0):
    np.random.seed(seed)
    _w = jnp.asarray

    def _rec_inputs():
        import jax
        import jax.numpy as jnp
        _tk = jax.random.key(seed)
        ids = jnp.stack([jax.random.randint(jax.random.fold_in(_tk, 200 + f), (512,), 0, v, jnp.int32) for f, v in enumerate([12500, 12500, 1000, 125000, 1250, 12500, 1250, 12500, 1250, 12500, 1000, 12500, 1000, 1000, 1250, 1000, 1000, 12500, 1250, 12500, 1250, 1250, 1250, 1250, 1000, 1000])], axis=1)
        tbl_0 = 0.05 * jax.random.normal(jax.random.fold_in(_tk, 500 + 0), (12500, 128), jnp.float32)
        tbl_1 = 0.05 * jax.random.normal(jax.random.fold_in(_tk, 500 + 1), (12500, 128), jnp.float32)
        tbl_2 = 0.05 * jax.random.normal(jax.random.fold_in(_tk, 500 + 2), (1000, 128), jnp.float32)
        tbl_3 = 0.05 * jax.random.normal(jax.random.fold_in(_tk, 500 + 3), (125000, 128), jnp.float32)
        tbl_4 = 0.05 * jax.random.normal(jax.random.fold_in(_tk, 500 + 4), (1250, 128), jnp.float32)
        tbl_5 = 0.05 * jax.random.normal(jax.random.fold_in(_tk, 500 + 5), (12500, 128), jnp.float32)
        tbl_6 = 0.05 * jax.random.normal(jax.random.fold_in(_tk, 500 + 6), (1250, 128), jnp.float32)
        tbl_7 = 0.05 * jax.random.normal(jax.random.fold_in(_tk, 500 + 7), (12500, 128), jnp.float32)
        tbl_8 = 0.05 * jax.random.normal(jax.random.fold_in(_tk, 500 + 8), (1250, 128), jnp.float32)
        tbl_9 = 0.05 * jax.random.normal(jax.random.fold_in(_tk, 500 + 9), (12500, 128), jnp.float32)
        tbl_10 = 0.05 * jax.random.normal(jax.random.fold_in(_tk, 500 + 10), (1000, 128), jnp.float32)
        tbl_11 = 0.05 * jax.random.normal(jax.random.fold_in(_tk, 500 + 11), (12500, 128), jnp.float32)
        tbl_12 = 0.05 * jax.random.normal(jax.random.fold_in(_tk, 500 + 12), (1000, 128), jnp.float32)
        tbl_13 = 0.05 * jax.random.normal(jax.random.fold_in(_tk, 500 + 13), (1000, 128), jnp.float32)
        tbl_14 = 0.05 * jax.random.normal(jax.random.fold_in(_tk, 500 + 14), (1250, 128), jnp.float32)
        tbl_15 = 0.05 * jax.random.normal(jax.random.fold_in(_tk, 500 + 15), (1000, 128), jnp.float32)
        tbl_16 = 0.05 * jax.random.normal(jax.random.fold_in(_tk, 500 + 16), (1000, 128), jnp.float32)
        tbl_17 = 0.05 * jax.random.normal(jax.random.fold_in(_tk, 500 + 17), (12500, 128), jnp.float32)
        tbl_18 = 0.05 * jax.random.normal(jax.random.fold_in(_tk, 500 + 18), (1250, 128), jnp.float32)
        tbl_19 = 0.05 * jax.random.normal(jax.random.fold_in(_tk, 500 + 19), (12500, 128), jnp.float32)
        tbl_20 = 0.05 * jax.random.normal(jax.random.fold_in(_tk, 500 + 20), (1250, 128), jnp.float32)
        tbl_21 = 0.05 * jax.random.normal(jax.random.fold_in(_tk, 500 + 21), (1250, 128), jnp.float32)
        tbl_22 = 0.05 * jax.random.normal(jax.random.fold_in(_tk, 500 + 22), (1250, 128), jnp.float32)
        tbl_23 = 0.05 * jax.random.normal(jax.random.fold_in(_tk, 500 + 23), (1250, 128), jnp.float32)
        tbl_24 = 0.05 * jax.random.normal(jax.random.fold_in(_tk, 500 + 24), (1000, 128), jnp.float32)
        tbl_25 = 0.05 * jax.random.normal(jax.random.fold_in(_tk, 500 + 25), (1000, 128), jnp.float32)
        _rk = jax.random.fold_in(_tk, 7)
        r_dense_features = -0.000520686 + 1.00062 * jax.random.normal(jax.random.fold_in(_rk, 101), (512, 128), jnp.float32)
        W_top1 = 0.0405887 * jax.random.normal(jax.random.fold_in(_tk, 801), (607, 512), jnp.float32)
        W_top2 = 0.0441942 * jax.random.normal(jax.random.fold_in(_tk, 802), (512, 256), jnp.float32)
        W_top3 = 0.0625 * jax.random.normal(jax.random.fold_in(_tk, 803), (256, 1), jnp.float32)
        b_top1 = jnp.zeros((512,), jnp.float32)
        b_top2 = jnp.zeros((256,), jnp.float32)
        return (r_dense_features, ids, tbl_0, tbl_1, tbl_2, tbl_3, tbl_4, tbl_5, tbl_6, tbl_7, tbl_8, tbl_9, tbl_10, tbl_11, tbl_12, tbl_13, tbl_14, tbl_15, tbl_16, tbl_17, tbl_18, tbl_19, tbl_20, tbl_21, tbl_22, tbl_23, tbl_24, tbl_25, W_top1, b_top1, W_top2, b_top2, W_top3)
    r_dense_features, ids, tbl_0, tbl_1, tbl_2, tbl_3, tbl_4, tbl_5, tbl_6, tbl_7, tbl_8, tbl_9, tbl_10, tbl_11, tbl_12, tbl_13, tbl_14, tbl_15, tbl_16, tbl_17, tbl_18, tbl_19, tbl_20, tbl_21, tbl_22, tbl_23, tbl_24, tbl_25, W_top1, b_top1, W_top2, b_top2, W_top3 = _rec_inputs()

    def _L0_rec_setup():
        import jax, jax.numpy as jnp
        import numpy as np
        F = 26
        key = jax.random.key(seed)
        k1, k2 = jax.random.split(key)
        B, D = (2048, 128)
        dense_features = jax.random.normal(k1, (B, D), dtype=jnp.float32)
        sparse_features = jax.random.normal(k2, (B, F, D), dtype=jnp.float32)
        return {'dense_features': dense_features, 'sparse_features': sparse_features}
    _L0_rec_all = _L0_rec_setup()
    _L0_rec_in = {k: v for k, v in _L0_rec_all.items() if k in ()}
    del _L0_rec_all
    return {'r_dense_features': r_dense_features, 'ids': ids, 'tbl_0': tbl_0, 'tbl_1': tbl_1, 'tbl_2': tbl_2, 'tbl_3': tbl_3, 'tbl_4': tbl_4, 'tbl_5': tbl_5, 'tbl_6': tbl_6, 'tbl_7': tbl_7, 'tbl_8': tbl_8, 'tbl_9': tbl_9, 'tbl_10': tbl_10, 'tbl_11': tbl_11, 'tbl_12': tbl_12, 'tbl_13': tbl_13, 'tbl_14': tbl_14, 'tbl_15': tbl_15, 'tbl_16': tbl_16, 'tbl_17': tbl_17, 'tbl_18': tbl_18, 'tbl_19': tbl_19, 'tbl_20': tbl_20, 'tbl_21': tbl_21, 'tbl_22': tbl_22, 'tbl_23': tbl_23, 'tbl_24': tbl_24, 'tbl_25': tbl_25, 'W_top1': W_top1, 'b_top1': b_top1, 'W_top2': W_top2, 'b_top2': b_top2, 'W_top3': W_top3}

def reference(r_dense_features, ids, tbl_0, tbl_1, tbl_2, tbl_3, tbl_4, tbl_5, tbl_6, tbl_7, tbl_8, tbl_9, tbl_10, tbl_11, tbl_12, tbl_13, tbl_14, tbl_15, tbl_16, tbl_17, tbl_18, tbl_19, tbl_20, tbl_21, tbl_22, tbl_23, tbl_24, tbl_25, W_top1, b_top1, W_top2, b_top2, W_top3):
    import jax
    import jax.numpy as jnp

    def _L0_rec_ref(dense_features, sparse_features):
        import jax, jax.numpy as jnp
        import numpy as np
        F = 26
        B, D = dense_features.shape
        combined = jnp.concatenate((dense_features[:, None, :], sparse_features), axis=1)
        interactions = jnp.einsum('bfd,bgd->bfg', combined, combined)
        iu, ju = jnp.triu_indices(F + 1, k=1)
        interactions_flat = interactions[:, iu, ju]
        return jnp.concatenate((dense_features, interactions_flat), axis=1)
    e = jnp.stack([tbl_0[ids[:, 0]], tbl_1[ids[:, 1]], tbl_2[ids[:, 2]], tbl_3[ids[:, 3]], tbl_4[ids[:, 4]], tbl_5[ids[:, 5]], tbl_6[ids[:, 6]], tbl_7[ids[:, 7]], tbl_8[ids[:, 8]], tbl_9[ids[:, 9]], tbl_10[ids[:, 10]], tbl_11[ids[:, 11]], tbl_12[ids[:, 12]], tbl_13[ids[:, 13]], tbl_14[ids[:, 14]], tbl_15[ids[:, 15]], tbl_16[ids[:, 16]], tbl_17[ids[:, 17]], tbl_18[ids[:, 18]], tbl_19[ids[:, 19]], tbl_20[ids[:, 20]], tbl_21[ids[:, 21]], tbl_22[ids[:, 22]], tbl_23[ids[:, 23]], tbl_24[ids[:, 24]], tbl_25[ids[:, 25]]], axis=1)
    z = _L0_rec_ref(r_dense_features, e)
    z = z.reshape(z.shape[0], -1)
    h = jnp.concatenate([z, r_dense_features], axis=1)
    h = jnp.maximum(h @ W_top1 + b_top1, 0.0)
    h = jnp.maximum(h @ W_top2 + b_top2, 0.0)
    y = h @ W_top3
    return y

_drawn_inputs = setup_inputs


def setup_inputs(seed=0):
    import zlib

    import numpy as np

    out = dict(_drawn_inputs(seed))
    spreads = {'b_top1': (0.0, 0.1), 'b_top2': (0.0, 0.1)}
    factors = {}
    for name, (base, spread) in spreads.items():
        noise = np.random.default_rng([zlib.crc32(name.encode()), seed]).standard_normal(out[name].shape)
        drawn = base * np.exp(spread * noise) if base else spread * noise
        out[name] = jnp.asarray(drawn.astype(out[name].dtype))
    for name, factor in factors.items():
        out[name] = (out[name] * factor).astype(out[name].dtype)
    return out
```

```python
from contextlib import ExitStack

import numpy as np

import concourse.bass as bass
from concourse import mybir

F32 = mybir.dt.float32
I32 = mybir.dt.int32
ALU = mybir.AluOpType
ACT = mybir.ActivationFunctionType

P = 128
BATCH = 512
D = 128
TABLES = 26
SLOTS = TABLES + 1
SLOT_PITCH = 32
HID1, HID2 = 512, 256
TILES = BATCH // P

QUADS = 4
GROUPS = P // QUADS
CHUNK = 4
CHUNKS = GROUPS // CHUNK
INTER_BANKS = 5

HALF = (SLOTS - 1) // 2
ROW_PITCH = 40
K_ROWS = 9
K_PAIRS = K_ROWS * HALF
K_TILES = SLOTS // K_ROWS

GATHERED = list(range(TABLES))
LOAD_GROUPS = [GATHERED[i:i + 4] for i in range(0, TABLES, 4)]
NG = len(LOAD_GROUPS)
NG_DVE = (NG + 1) // 2
NG_ACT = NG // 2


def build(nc, dense_t, ids, tables, w1_pairs, w1_dense, w2, columns, out):
    with ExitStack() as ctx:
        def sb(name, shape, dt=F32):
            return ctx.enter_context(nc.sbuf_tensor(name, shape, dt))

        def sem(name):
            return ctx.enter_context(nc.semaphore(name))

        ids_sb = sb("ids_sb", [P, TILES, TABLES], I32)
        emb = sb("emb", [P, TABLES, D])
        ident = sb("ident", [P, P])
        dense_sb = sb("dense_sb", [D, BATCH])
        xT = sb("xT", [D, GROUPS, QUADS, SLOT_PITCH])
        inter = sb("inter", [P, SLOTS, GROUPS])
        inter_s = sb("inter_s", [P, SLOTS * (ROW_PITCH + 1) + 1])
        pairs_s = sb("pairs_s", [P, K_TILES, K_PAIRS])
        pairs = sb("pairs", [P, K_TILES, P])
        w1p_sb = sb("w1p_sb", [P, K_TILES, HID1])
        w1d_sb = sb("w1d_sb", [P, 2, HID1])
        w1_sum = sb("w1_sum", [P, HID1])
        w2_sb = sb("w2_sb", [P, HID1 // P, HID2])
        col_sb = sb("col_sb", [P, 8])
        h1 = sb("h1", [P, HID1 // P, P])
        h2 = sb("h2", [P, HID2 // P, P])
        y_row = sb("y_row", [1, BATCH])

        bank = [ctx.enter_context(nc.psum_tensor(f"bank{i}", [P, 512], F32)) for i in range(8)]
        t_bank = bank[0:2]
        i_bank = bank[2:2 + INTER_BANKS]
        h2_bank = [bank[7], i_bank[3]]
        y_bank = i_bank[4]

        s_ids = sem("s_ids")
        s_dense = sem("s_dense")
        s_w1p = sem("s_w1p")
        s_w1d = sem("s_w1d")
        s_w2 = sem("s_w2")
        s_col = sem("s_col")
        s_zero = sem("s_zero")
        s_ident = sem("s_ident")
        s_pad = sem("s_pad")
        s_w1sum = sem("s_w1sum")
        s_gather = [sem(f"s_gather{g}") for g in range(NG)]
        s_tr = sem("s_tr")
        s_resident = sem("s_resident")
        s_xt_dve = sem("s_xt_dve")
        s_xt_act = sem("s_xt_act")
        s_prod = sem("s_prod")
        s_take_dve = sem("s_take_dve")
        s_take_act = sem("s_take_act")
        s_blk = sem("s_blk")
        s_wrap = sem("s_wrap")
        s_pick_dve = sem("s_pick_dve")
        s_pick_act = sem("s_pick_act")
        s_ptr = sem("s_ptr")
        s_pair_dve = sem("s_pair_dve")
        s_pair_act = sem("s_pair_act")
        s_l1 = sem("s_l1")
        s_h1_act = sem("s_h1_act")
        s_h1_dve = sem("s_h1_dve")
        s_l2 = sem("s_l2")
        s_h2_act = sem("s_h2_act")
        s_h2_dve = sem("s_h2_dve")
        s_l3 = sem("s_l3")
        s_y = sem("s_y")
        s_out = sem("s_out")

        blocks = inter_s[:, 0:SLOTS * ROW_PITCH].rearrange("s (g f) -> s g f", f=ROW_PITCH)

        def partners(k):
            first = (ROW_PITCH + 1) * K_ROWS * k + 1
            rows = inter_s[:, first:first + K_ROWS * (ROW_PITCH + 1)]
            return rows.rearrange("s (g f) -> s g f", g=K_ROWS)[:, :, 0:HALF]

        def picked(k):
            return pairs_s[:, k, :].rearrange("s (g f) -> s g f", g=K_ROWS)

        def group_psum(g):
            n = len(LOAD_GROUPS[g])
            return t_bank[g % 2][:, 0:n * P].rearrange("d (f q j) -> d q j f", f=n, q=QUADS)

        def group_slots(g):
            first = LOAD_GROUPS[g][0] + 1
            return xT[:, :, :, first:first + len(LOAD_GROUPS[g])].rearrange("d j q f -> d q j f")

        def block_of(c, q):
            rows = slice(32 * q, 32 * q + 32)
            width = QUADS * SLOTS
            src = i_bank[c % INTER_BANKS][rows, 0:CHUNK * width].rearrange("p (j n) -> p j n", j=CHUNK)
            src = src[:, :, q * SLOTS:(q + 1) * SLOTS].rearrange("p j g -> p g j")
            return inter[rows, :, CHUNK * c:CHUNK * (c + 1)], src

        block = ctx.enter_context(nc.Block())

        @block.sync
        def _(sp):
            sp.dma_start(ids_sb[:], ids.rearrange("(t s) f -> s t f", s=P)).then_inc(s_ids, 16)
            sp.dma_start(dense_sb[:], dense_t).then_inc(s_dense, 16)
            sp.dma_start(w1d_sb[:], w1_dense.rearrange("(c p) n -> p c n", p=P)).then_inc(s_w1d, 16)
            sp.dma_start(w1p_sb[0:K_PAIRS], w1_pairs.rearrange("(k p) n -> p k n", p=K_PAIRS)).then_inc(s_w1p, 16)
            sp.dma_start(w2_sb[:], w2.rearrange("(c p) n -> p c n", p=P)).then_inc(s_w2, 16)
            sp.dma_start(col_sb[:], columns).then_inc(s_col, 16)
            sp.wait_ge(s_y, TILES)
            sp.dma_start(out.rearrange("b o -> o b"), y_row[:]).then_inc(s_out, 16)
            sp.wait_ge(s_out, 16)

        @block.gpsimd
        def _(pool):
            nc.gpsimd.memset(ident[:], 0.0).then_inc(s_zero, 1)
            pool.wait_ge(s_zero, 1)
            nc.gpsimd.affine_select(out=ident[:], in_=ident[:], compare_op=ALU.not_equal, fill=1.0, base=0,
                                    pattern=[[-1, P]], channel_multiplier=1).then_inc(s_ident, 1)
            pool.wait_ge(s_ids, 16)
            for t in range(TILES):
                for g, group in enumerate(LOAD_GROUPS):
                    if t >= 1:
                        pool.wait_ge(s_tr, NG * (t - 1) + g + 1)
                    for f in group:
                        nc.gpsimd.indirect_dma_start(
                            out=emb[:, f, :], out_offset=None, in_=tables[f],
                            in_offset=bass.IndirectOffsetOnAxis(ap=ids_sb[:, t, f:f + 1], axis=0),
                        ).then_inc(s_gather[g], 16)

        @block.tensor
        def _(pe):
            pe.wait_ge(s_ident, 1)
            def tile(t, first):
                for g, group in enumerate(LOAD_GROUPS):
                    if g < 2 and first:
                        pass
                    elif g == 0:
                        pe.wait_ge(s_h1_act, t)
                    elif g == 1:
                        pe.wait_ge(s_h1_dve, t)
                    elif g % 2 == 0:
                        pe.wait_ge(s_xt_dve, t * NG_DVE + g // 2)
                    else:
                        pe.wait_ge(s_xt_act, t * NG_ACT + g // 2)
                    pe.wait_ge(s_gather[g], (t + 1) * (16 * len(group)))
                    for i, f in enumerate(group):
                        mm = nc.tensor.transpose(t_bank[g % 2][:, i * P:(i + 1) * P], emb[:, f, :], ident[:])
                    mm.then_inc(s_tr, 1)

                pe.wait_ge(s_pad, 1)
                pe.wait_ge(s_resident, t + 1)
                pe.wait_ge(s_xt_dve, (t + 1) * NG_DVE)
                pe.wait_ge(s_xt_act, (t + 1) * NG_ACT)
                if not first:
                    pe.wait_ge(s_y, t)
                for c in range(CHUNKS):
                    if c >= INTER_BANKS:
                        pe.wait_ge(s_take_dve, t * CHUNKS + c - INTER_BANKS + 1)
                        pe.wait_ge(s_take_act, t * CHUNKS + c - INTER_BANKS + 1)
                    for i in range(CHUNK):
                        j = c * CHUNK + i
                        width = QUADS * SLOTS
                        mm = nc.tensor.matmul(i_bank[c % INTER_BANKS][:, i * width:(i + 1) * width],
                                              xT[:, j, :, :].rearrange("d q f -> d (q f)"), xT[:, j, :, 0:SLOTS],
                                              start=True, stop=True)
                    mm.then_inc(s_prod, 1)

                for k in range(K_TILES):
                    if k == K_TILES - 1:
                        pe.wait_ge(s_pick_dve, t + 1)
                    else:
                        pe.wait_ge(s_pick_act, t * 2 + k + 1)
                    nc.tensor.transpose(i_bank[k][0:K_PAIRS, 0:P], pairs_s[:, k, :], ident[:]).then_inc(s_ptr, 1)

                pe.wait_ge(s_w1sum, 1)
                pe.wait_ge(s_w1p, 16)
                pe.wait_ge(s_pair_dve, (t + 1) * 2)
                pe.wait_ge(s_pair_act, t + 1)
                for n in range(HID1 // P):
                    dst = t_bank[n // 2][:, (n % 2) * P:(n % 2 + 1) * P]
                    cols = slice(n * P, (n + 1) * P)
                    nc.tensor.matmul(dst, w1_sum[:, cols], dense_sb[:, bass.ts(t, P)], start=True, stop=False)
                    for k in range(K_TILES):
                        mm = nc.tensor.matmul(dst, w1p_sb[0:K_PAIRS, k, cols], pairs[0:K_PAIRS, k, :],
                                              start=False, stop=(k == K_TILES - 1))
                    if n % 2:
                        mm.then_inc(s_l1, 1)

                pe.wait_ge(s_w2, 16)
                pe.wait_ge(s_h1_act, t + 1)
                pe.wait_ge(s_h1_dve, t + 1)
                for m in range(HID2 // P):
                    for c in range(HID1 // P):
                        mm = nc.tensor.matmul(h2_bank[m][:, 0:P], w2_sb[:, c, m * P:(m + 1) * P], h1[:, c, :],
                                              start=(c == 0), stop=(c == HID1 // P - 1))
                    mm.then_inc(s_l2, 1)

                pe.wait_ge(s_h2_act, t + 1)
                pe.wait_ge(s_h2_dve, t + 1)
                for m in range(HID2 // P):
                    mm = nc.tensor.matmul(y_bank[0:1, 0:P], col_sb[:, 6 + m:7 + m], h2[:, m, :],
                                          start=(m == 0), stop=(m == HID2 // P - 1))
                mm.then_inc(s_l3, 1)

            tile(0, True)
            with pe.Fori(1, TILES) as t:
                tile(t, False)

        @block.vector
        def _(dve):
            nc.vector.memset(xT[:, :, :, SLOTS:SLOT_PITCH], 0.0).then_inc(s_pad, 1)
            dve.wait_ge(s_w1d, 16)
            nc.vector.tensor_tensor(w1_sum[:], w1d_sb[:, 0, :], w1d_sb[:, 1, :], ALU.add).then_inc(s_w1sum, 1)
            dve.wait_ge(s_col, 16)
            def tile(t, first):
                for g in range(0, NG, 2):
                    dve.wait_ge(s_tr, t * NG + g + 1)
                    nc.vector.tensor_copy(group_slots(g), group_psum(g)).then_inc(s_xt_dve, 1)
                for c in range(CHUNKS):
                    dve.wait_ge(s_prod, t * CHUNKS + c + 1)
                    for q in (0, 1):
                        take = nc.vector.tensor_copy(*block_of(c, q))
                    take.then_inc(s_take_dve, 1)
                dve.wait_ge(s_take_dve, (t + 1) * CHUNKS)
                dve.wait_ge(s_take_act, (t + 1) * CHUNKS)
                if not first:
                    dve.wait_ge(s_pick_act, t * 2)
                nc.vector.transpose(blocks[:, :, 0:GROUPS], inter[:]).then_inc(s_blk, 1)
                dve.wait_ge(s_blk, t + 1)
                nc.vector.tensor_copy(blocks[:, SLOTS - HALF:SLOTS, SLOTS:SLOTS + HALF],
                                      blocks[:, SLOTS - HALF:SLOTS, 0:HALF]).then_inc(s_wrap, 1)
                dve.wait_ge(s_wrap, t + 1)
                nc.vector.tensor_copy(picked(2), partners(2)).then_inc(s_pick_dve, 1)
                for k in (0, 2):
                    dve.wait_ge(s_ptr, t * K_TILES + k + 1)
                    nc.vector.tensor_copy(pairs[0:K_PAIRS, k, :], i_bank[k][0:K_PAIRS, 0:P]).then_inc(s_pair_dve, 1)
                dve.wait_ge(s_l1, t * 2 + 2)
                for n in (2, 3):
                    relu = nc.vector.tensor_scalar(h1[:, n, :], t_bank[1][:, (n - 2) * P:(n - 1) * P],
                                                   col_sb[:, n:n + 1], 0.0, ALU.add, ALU.max)
                relu.then_inc(s_h1_dve, 1)
                dve.wait_ge(s_l2, t * 2 + 2)
                nc.vector.tensor_scalar(h2[:, 1, :], h2_bank[1][:, 0:P], col_sb[:, 5:6], 0.0,
                                        ALU.add, ALU.max).then_inc(s_h2_dve, 1)

            tile(0, True)
            with dve.Fori(1, TILES) as t:
                tile(t, False)

        @block.scalar
        def _(act):
            act.wait_ge(s_dense, 16)
            act.wait_ge(s_col, 16)
            def tile(t, first):
                if not first:
                    act.wait_ge(s_prod, t * CHUNKS)
                nc.scalar.copy(xT[:, :, :, 0].rearrange("d j q -> d q j"),
                               dense_sb[:, bass.ts(t, P)].rearrange("d (q j) -> d q j", q=QUADS)).then_inc(s_resident, 1)
                for g in range(1, NG, 2):
                    act.wait_ge(s_tr, t * NG + g + 1)
                    nc.scalar.copy(group_slots(g), group_psum(g)).then_inc(s_xt_act, 1)
                if not first:
                    act.wait_ge(s_blk, t)
                for c in range(CHUNKS):
                    act.wait_ge(s_prod, t * CHUNKS + c + 1)
                    for q in (2, 3):
                        take = nc.scalar.copy(*block_of(c, q))
                    take.then_inc(s_take_act, 1)
                for k in (0, 1):
                    if k == 0:
                        act.wait_ge(s_blk, t + 1)
                    else:
                        act.wait_ge(s_wrap, t + 1)
                    nc.scalar.copy(picked(k), partners(k)).then_inc(s_pick_act, 1)
                act.wait_ge(s_ptr, t * K_TILES + 2)
                nc.scalar.copy(pairs[0:K_PAIRS, 1, :], i_bank[1][0:K_PAIRS, 0:P]).then_inc(s_pair_act, 1)
                act.wait_ge(s_l1, t * 2 + 1)
                for n in (0, 1):
                    relu = nc.scalar.activation(h1[:, n, :], t_bank[0][:, n * P:(n + 1) * P], ACT.Relu,
                                                bias=col_sb[:, n:n + 1])
                relu.then_inc(s_h1_act, 1)
                act.wait_ge(s_l2, t * 2 + 1)
                nc.scalar.activation(h2[:, 0, :], h2_bank[0][:, 0:P], ACT.Relu,
                                     bias=col_sb[:, 4:5]).then_inc(s_h2_act, 1)
                act.wait_ge(s_l3, t + 1)
                nc.scalar.copy(y_row[0:1, bass.ts(t, P)], y_bank[0:1, 0:P]).then_inc(s_y, 1)

            tile(0, True)
            with act.Fori(1, TILES) as t:
                tile(t, False)


def kernel(**inputs):
    import concourse.bacc as bacc
    from concourse.bass_utils import run_bass_kernel_spmd

    row_of = {}
    for a in range(SLOTS):
        for b in range(a + 1, SLOTS):
            row_of[a, b] = D + len(row_of)
    order = []
    for g in range(SLOTS):
        for k in range(1, HALF + 1):
            b = (g + k) % SLOTS
            order.append(row_of[min(g, b), max(g, b)])

    w1 = np.asarray(inputs["W_top1"])
    last = w1.shape[0] - D
    arrays = {
        "dense_t": np.asarray(inputs["r_dense_features"]).T,
        "ids": inputs["ids"],
        **{f"tbl_{f}": inputs[f"tbl_{f}"] for f in range(TABLES)},
        "w1_pairs": w1[order],
        "w1_dense": np.concatenate([w1[:D], w1[last:]]),
        "w2": inputs["W_top2"],
        "columns": np.concatenate([np.asarray(inputs["b_top1"]).reshape(-1, P), np.asarray(inputs["b_top2"]).reshape(-1, P),
                                   np.asarray(inputs["W_top3"]).reshape(-1, P)]).T,
    }
    nc = bacc.Bacc("TRN2", target_bir_lowering=False, num_devices=1)
    sent, aps = {}, {}
    for name, a in arrays.items():
        a = np.ascontiguousarray(a)
        sent[f"in_{name}"] = a
        aps[name] = nc.dram_tensor(f"in_{name}", a.shape, mybir.dt.from_np(a.dtype), kind="ExternalInput").ap()
    out = nc.dram_tensor("out_y", (BATCH, 1), F32, kind="ExternalOutput").ap()
    build(nc, aps["dense_t"], aps["ids"], [aps[f"tbl_{f}"] for f in range(TABLES)], aps["w1_pairs"],
          aps["w1_dense"], aps["w2"], aps["columns"], out)
    r = run_bass_kernel_spmd(nc, [sent], core_ids=[0])
    return r.results[0]["out_y"]
```

```python
from contextlib import ExitStack

import numpy as np

import concourse.bass as bass
from concourse import mybir

F32 = mybir.dt.float32
F16 = mybir.dt.float16
BF16 = mybir.dt.bfloat16
I32 = mybir.dt.int32
ALU = mybir.AluOpType
ACT = mybir.ActivationFunctionType

P = 128
BATCH = 512
D = 128
TABLES = 26
SLOTS = TABLES + 1
SLOT_PITCH = 32
HID1, HID2 = 512, 256
TILES = BATCH // P

RESIDENT = 5
GATHERED = TABLES - RESIDENT
GROUP = 4
LOAD_GROUPS = [range(f, min(f + GROUP, GATHERED)) for f in range(0, GATHERED, GROUP)]
NG = len(LOAD_GROUPS)
T_BANKS = 5
ROWS_PER_PART = 8
MAX_RESIDENT_ROWS = 2048
LATE = 3

QUADS = 4
MATMULS = P // QUADS
CHUNK = 4
CHUNKS = MATMULS // CHUNK
PROD_BANKS = 5
PROD_W = QUADS * SLOTS

HALF = (SLOTS - 1) // 2
ROW_PITCH = 40
K_ROWS = 9
K_PAIRS = K_ROWS * HALF
K_TILES = SLOTS // K_ROWS

AFTER_DENSE, AFTER_PAIRS, AFTER_LAYER1, AFTER_LAYER2 = range(4)
FILL = [[0, 1, 2, 3]] * (TILES - 2) + [[0]]

LOOKUPS = [(r, slice(0, BATCH if r < RESIDENT - LATE else BATCH - P)) for r in range(RESIDENT)]
LOOKUPS += [(r, slice(BATCH - P, BATCH)) for r in range(RESIDENT - LATE, RESIDENT)]

LATE_AFTER = {1: RESIDENT, 2: RESIDENT + 1, 3: RESIDENT + 2}

B1, B2, W3, ROW_ID = 0, HID1 // P, HID1 // P + HID2 // P, HID1 // P + 2 * (HID2 // P)
N_COLS = ROW_ID + ROWS_PER_PART


def build(nc, dense_t, ids, resident_ids, resident, gathered, w1_pairs, w1_dense, w2, columns, out):
    part_rows = resident[0].shape[0] // ROWS_PER_PART
    assert all(t.shape[0] == part_rows * ROWS_PER_PART <= MAX_RESIDENT_ROWS for t in resident)
    assert part_rows <= P

    with ExitStack() as ctx:
        def sb(name, shape, dt=F32):
            return ctx.enter_context(nc.sbuf_tensor(name, shape, dt))

        def sem(name):
            return ctx.enter_context(nc.semaphore(name))

        ids_sb = sb("ids_sb", [P, TILES, GATHERED], I32)
        emb = sb("emb", [P, 2, GATHERED, D])
        ident = sb("ident", [P, P])
        table = sb("table", [part_rows, RESIDENT, ROWS_PER_PART * D])
        rest = sb("rest", [part_rows, LATE, ROWS_PER_PART * D])
        low = sb("low", [part_rows, LATE, ROWS_PER_PART, D], BF16)
        ids_i = sb("ids_i", [part_rows, RESIDENT, BATCH], I32)
        ids_h = sb("ids_h", [part_rows, 2, BATCH], F16)
        mask = sb("mask", [part_rows, LATE, ROWS_PER_PART, BATCH], BF16)
        known = sb("known", [D, 1 + RESIDENT, BATCH])
        xT = sb("xT", [D, 2, MATMULS, QUADS, SLOT_PITCH])
        inter = sb("inter", [P, SLOTS, MATMULS])
        inter_s = sb("inter_s", [P, SLOTS * (ROW_PITCH + 1) + 1])
        pairs_s = sb("pairs_s", [P, K_TILES, K_PAIRS])
        pairs = sb("pairs", [P, K_TILES, P])
        w1p_sb = sb("w1p_sb", [P, K_TILES, HID1])
        w1d_sb = sb("w1d_sb", [P, 2, HID1])
        w1_sum = sb("w1_sum", [P, HID1])
        w2_sb = sb("w2_sb", [P, HID1 // P, HID2])
        col_sb = sb("col_sb", [P, N_COLS])
        h1 = sb("h1", [P, HID1 // P, P])
        h2 = sb("h2", [P, HID2 // P, P])
        first = sb("first", [1, 2])
        y_row = sb("y_row", [1, BATCH])

        bank = [ctx.enter_context(nc.psum_tensor(f"bank{i}", [P, 512], F32)) for i in range(8)]
        p_bank = bank[2:2 + PROD_BANKS]
        look_bank = [p_bank[0], p_bank[1]]
        t_bank = [p_bank[3], p_bank[4], bank[7], bank[0], bank[1]]
        pt_bank = p_bank[0:K_TILES]
        l1_bank = [bank[0], bank[1]]
        l2_bank = [p_bank[0], p_bank[1]]
        y_bank = p_bank[2]

        s_ids = sem("s_ids")
        s_idb = [sem(f"s_idb{r}") for r in range(RESIDENT)]
        s_table = [sem(f"s_table{r}") for r in range(RESIDENT)]
        s_dense = sem("s_dense")
        s_w1p = sem("s_w1p")
        s_w1d = sem("s_w1d")
        s_w2 = sem("s_w2")
        s_col = sem("s_col")
        s_gather = [[sem(f"s_gather{b}_{g}") for g in range(NG)] for b in range(2)]
        s_first = sem("s_first")
        s_zero = sem("s_zero")
        s_ident = sem("s_ident")
        s_pad = sem("s_pad")
        s_w1sum = sem("s_w1sum")
        s_idh = sem("s_idh")
        s_mask = sem("s_mask")
        s_rest = sem("s_rest")
        s_low = sem("s_low")
        s_look = sem("s_look")
        s_known = sem("s_known")
        s_tr = sem("s_tr")
        s_pack = [sem(f"s_pack{g}") for g in range(NG)]
        s_pack_known = sem("s_pack_known")
        s_prod = sem("s_prod")
        s_take_dve = sem("s_take_dve")
        s_take_act = sem("s_take_act")
        s_blk = sem("s_blk")
        s_wrap = sem("s_wrap")
        s_pick_dve = sem("s_pick_dve")
        s_pick_act = sem("s_pick_act")
        s_ptr = sem("s_ptr")
        s_pair_dve = sem("s_pair_dve")
        s_pair_act = sem("s_pair_act")
        s_l1 = sem("s_l1")
        s_h1_act = sem("s_h1_act")
        s_h1_dve = sem("s_h1_dve")
        s_l2 = sem("s_l2")
        s_h2_act = sem("s_h2_act")
        s_h2_dve = sem("s_h2_dve")
        s_l3 = sem("s_l3")
        s_y = sem("s_y")
        s_out = sem("s_out")

        blocks = inter_s[:, 0:SLOTS * ROW_PITCH].rearrange("s (g f) -> s g f", f=ROW_PITCH)

        def upper_halves(words):
            return words.bitcast(BF16).rearrange("p (k d two) -> p k d two", k=ROWS_PER_PART, two=2)[:, :, :, 1]

        def by_row(words):
            return words.rearrange("p (k d) -> p k d", k=ROWS_PER_PART)

        def partners(k):
            first = (ROW_PITCH + 1) * K_ROWS * k + 1
            rows = inter_s[:, first:first + K_ROWS * (ROW_PITCH + 1)]
            return rows.rearrange("s (g f) -> s g f", g=K_ROWS)[:, :, 0:HALF]

        def picked(k):
            return pairs_s[:, k, :].rearrange("s (g f) -> s g f", g=K_ROWS)

        def slots(t, first, n):
            return xT[:, t % 2, :, :, first:first + n].rearrange("d j q f -> d q j f")

        def pack(t, g):
            n = len(LOAD_GROUPS[g])
            return (slots(t, 1 + RESIDENT + LOAD_GROUPS[g].start, n),
                    t_bank[g % T_BANKS][:, 0:n * P].rearrange("d (f q j) -> d q j f", f=n, q=QUADS))

        def take(c, q):
            rows = slice(32 * q, 32 * q + 32)
            src = p_bank[c % PROD_BANKS][rows, 0:CHUNK * PROD_W].rearrange("p (j n) -> p j n", j=CHUNK)
            src = src[:, :, q * SLOTS:(q + 1) * SLOTS].rearrange("p j g -> p g j")
            return inter[rows, :, CHUNK * c:CHUNK * (c + 1)], src

        block = ctx.enter_context(nc.Block())

        @block.sync
        def _(sp):
            sp.dma_start(ids_sb[:], ids.rearrange("(t s) f -> s t f", s=P)).then_inc(s_ids, 16)
            for r in range(RESIDENT):
                if r >= 1:
                    sp.dma_start(ids_i[:, r, :], resident_ids[r].partition_broadcast(part_rows)).then_inc(s_idb[r], 16)
                sp.dma_start(table[:, r, :], resident[r].rearrange("(p k) d -> p (k d)", k=ROWS_PER_PART)
                             ).then_inc(s_table[r], 16)
            sp.dma_start(known[:, 0, :], dense_t).then_inc(s_dense, 16)
            sp.dma_start(w1d_sb[:], w1_dense.rearrange("(c p) n -> p c n", p=P)).then_inc(s_w1d, 16)
            sp.dma_start(w1p_sb[0:K_PAIRS], w1_pairs.rearrange("(k p) n -> p k n", p=K_PAIRS)).then_inc(s_w1p, 16)
            sp.dma_start(w2_sb[:], w2.rearrange("(c p) n -> p c n", p=P)).then_inc(s_w2, 16)
            sp.wait_ge(s_y, TILES)
            sp.dma_start(out.rearrange("b o -> o b"), y_row[:]).then_inc(s_out, 16)
            sp.wait_ge(s_out, 16)

        @block.gpsimd
        def _(pool):
            nc.gpsimd.memset(ident[:], 0.0).then_inc(s_zero, 1)
            pool.wait_ge(s_zero, 1)
            nc.gpsimd.affine_select(out=ident[:], in_=ident[:], compare_op=ALU.not_equal, fill=1.0, base=0,
                                    pattern=[[-1, P]], channel_multiplier=1).then_inc(s_ident, 1)
            pool.wait_ge(s_ids, 16)
            for t in range(TILES):
                for g in range(NG):
                    if t >= 2:
                        pool.wait_ge(s_tr, NG * (t - 2) + g + 1)
                    for f in LOAD_GROUPS[g]:
                        nc.gpsimd.indirect_dma_start(
                            out=emb[:, t % 2, f, :], out_offset=None, in_=gathered[f],
                            in_offset=bass.IndirectOffsetOnAxis(ap=ids_sb[:, t, f:f + 1], axis=0),
                        ).then_inc(s_gather[t % 2][g], 16)

        @block.tensor
        def _(pe):
            def look_up(n):
                r, samples = LOOKUPS[n]
                dst = look_bank[n % 2][:, 0:samples.stop - samples.start]
                if n >= 2:
                    pe.wait_ge(s_known, n - 1)
                pe.wait_ge(s_table[r], 16)
                for part in range(3):
                    if part == 1:
                        pe.wait_ge(s_rest, r + 1)
                    if part == 2:
                        pe.wait_ge(s_low, r + 1)
                    src = [upper_halves(table[:, r, :]), upper_halves(rest[:, r % LATE, :]), low[:, r % LATE]][part]
                    for k in range(ROWS_PER_PART):
                        if part == 0:
                            pe.wait_ge(s_mask, r * ROWS_PER_PART + k + 1)
                        mm = nc.tensor.matmul(dst, src[:, k, :], mask[:, r % LATE, k, samples],
                                              start=(part == 0 and k == 0),
                                              stop=(part == 2 and k == ROWS_PER_PART - 1))
                mm.then_inc(s_look, 1)

            def turn(t, g):
                if t >= 1 and g in (0, 1):
                    pe.wait_ge(s_take_dve, (t - 1) * CHUNKS + g + 4)
                    pe.wait_ge(s_take_act, (t - 1) * CHUNKS + g + 4)
                if t >= 1 and g in (3, 4):
                    pe.wait_ge((s_h1_act, s_h1_dve)[g - 3], t)
                if g >= T_BANKS:
                    pe.wait_ge(s_pack[g - T_BANKS], t + 1)
                pe.wait_ge(s_gather[t % 2][g], (t // 2 + 1) * 16 * len(LOAD_GROUPS[g]))
                for i, f in enumerate(LOAD_GROUPS[g]):
                    mm = nc.tensor.transpose(t_bank[g % T_BANKS][:, i * P:(i + 1) * P],
                                             emb[:, t % 2, f, :], ident[:])
                mm.then_inc(s_tr, 1)

            def fill(t, place):
                if t + 1 < TILES and place < len(FILL[t]):
                    turn(t + 1, FILL[t][place])

            def interact(t):
                pe.wait_ge(s_pad, 1)
                pe.wait_ge(s_pack_known, t + 1)
                for g in range(NG):
                    pe.wait_ge(s_pack[g], t + 1)
                if t >= 1:
                    pe.wait_ge(s_y, t)
                for c in range(CHUNKS):
                    if c >= PROD_BANKS:
                        pe.wait_ge(s_take_dve, t * CHUNKS + c - PROD_BANKS + 1)
                        pe.wait_ge(s_take_act, t * CHUNKS + c - PROD_BANKS + 1)
                    for i in range(CHUNK):
                        x = xT[:, t % 2, c * CHUNK + i, :, :]
                        mm = nc.tensor.matmul(p_bank[c % PROD_BANKS][:, i * PROD_W:(i + 1) * PROD_W],
                                              x.rearrange("d q f -> d (q f)"), x[:, :, 0:SLOTS],
                                              start=True, stop=True)
                    mm.then_inc(s_prod, 1)

            def pair_rows(t, k, layer1):
                if k == K_TILES - 1:
                    pe.wait_ge(s_pair_dve, t + 1)
                else:
                    pe.wait_ge(s_pair_act, t * 2 + k + 1)
                for n in range(HID1 // P):
                    mm = layer1(n, w1p_sb[0:K_PAIRS, k, :], pairs[0:K_PAIRS, k, :], k == K_TILES - 1)
                    if k == K_TILES - 1 and n % 2:
                        mm.then_inc(s_l1, 1)

            def mlp(t):
                pe.wait_ge(s_w1sum, 1)
                pe.wait_ge(s_w1p, 16)

                def layer1(n, weights, x, last):
                    return nc.tensor.matmul(l1_bank[n // 2][:, (n % 2) * P:(n % 2 + 1) * P],
                                            weights[:, n * P:(n + 1) * P], x,
                                            start=(weights is w1_sum and n % 2 == 0), stop=last,
                                            skip_group_check=True)

                for n in range(HID1 // P):
                    layer1(n, w1_sum, known[:, 0, t * P:(t + 1) * P], False)
                fill(t, AFTER_DENSE)
                for k in range(K_TILES):
                    if k == K_TILES - 1:
                        pe.wait_ge(s_pick_dve, t + 1)
                    else:
                        pe.wait_ge(s_pick_act, t * 2 + k + 1)
                    nc.tensor.transpose(pt_bank[k][0:K_PAIRS, 0:P], pairs_s[:, k, :], ident[:]).then_inc(s_ptr, 1)
                    if k == 0:
                        fill(t, AFTER_PAIRS)
                        pair_rows(t, k, layer1)
                for k in range(1, K_TILES):
                    pair_rows(t, k, layer1)
                fill(t, AFTER_LAYER1)
                pe.wait_ge(s_w2, 16)
                pe.wait_ge(s_h1_act, t + 1)
                for m in range(HID2 // P):
                    for c in range(HID1 // P):
                        if m == 0 and c == 2:
                            pe.wait_ge(s_h1_dve, t + 1)
                        mm = nc.tensor.matmul(l2_bank[m][:, 0:P], w2_sb[:, c, m * P:(m + 1) * P], h1[:, c, :],
                                              start=(c == 0), stop=(c == HID1 // P - 1))
                    mm.then_inc(s_l2, 1)
                fill(t, AFTER_LAYER2)
                for m in range(HID2 // P):
                    pe.wait_ge((s_h2_act, s_h2_dve)[m], t + 1)
                    mm = nc.tensor.matmul(y_bank[0:1, 0:P], col_sb[:, W3 + m:W3 + m + 1], h2[:, m, :],
                                          start=(m == 0), stop=(m == HID2 // P - 1))
                mm.then_inc(s_l3, 1)

            for r in range(RESIDENT - 1):
                look_up(r)
            pe.wait_ge(s_ident, 1)
            for g in range(NG):
                turn(0, g)
            look_up(RESIDENT - 1)
            for t in range(TILES):
                interact(t)
                mlp(t)
                if t + 1 < TILES:
                    for g in range(len(FILL[t]), NG):
                        turn(t + 1, g)
                        if t + 1 == TILES - 1 and g in LATE_AFTER:
                            look_up(LATE_AFTER[g])

        @block.vector
        def _(dve):
            def pack_group(t, g):
                dve.wait_ge(s_tr, t * NG + g + 1)
                if t >= 2:
                    dve.wait_ge(s_prod, (t - 1) * CHUNKS)
                nc.vector.tensor_copy(*pack(t, g)).then_inc(s_pack[g], 1)

            def fill(t, place):
                if t + 1 < TILES and place < len(FILL[t]):
                    pack_group(t + 1, FILL[t][place])

            nc.vector.memset(first[:], 0.0).then_inc(s_first, 1)
            dve.wait_ge(s_col, 16)
            for r in range(RESIDENT):
                dve.wait_ge(s_idh, r + 1)
                if r >= LATE:
                    dve.wait_ge(s_look, r - LATE + 1)
                for k in range(ROWS_PER_PART):
                    nc.vector.tensor_scalar(mask[:, r % LATE, k, :], ids_h[:, r % 2, :],
                                            col_sb[0:part_rows, ROW_ID + k:ROW_ID + k + 1], None,
                                            ALU.is_equal).then_inc(s_mask, 1)
                dve.wait_ge(s_table[r], 16)
                nc.vector.tensor_tensor(by_row(rest[:, r % LATE, :]), by_row(table[:, r, :]),
                                        upper_halves(table[:, r, :]), ALU.subtract).then_inc(s_rest, 1)
                dve.wait_ge(s_rest, r + 1)
                nc.vector.tensor_tensor(low[:, r % LATE], by_row(rest[:, r % LATE, :]),
                                        upper_halves(rest[:, r % LATE, :]), ALU.subtract).then_inc(s_low, 1)
            for b in range(2):
                pad = nc.vector.memset(xT[:, b, :, :, SLOTS:SLOT_PITCH], 0.0)
            pad.then_inc(s_pad, 1)
            for g in range(0, NG, 2):
                pack_group(0, g)
            dve.wait_ge(s_w1d, 16)
            nc.vector.tensor_tensor(w1_sum[:], w1d_sb[:, 0, :], w1d_sb[:, 1, :], ALU.add).then_inc(s_w1sum, 1)

            for t in range(TILES):
                for c in range(CHUNKS):
                    dve.wait_ge(s_prod, t * CHUNKS + c + 1)
                    for q in (0, 1):
                        last = nc.vector.tensor_copy(*take(c, q))
                    last.then_inc(s_take_dve, 1)
                dve.wait_ge(s_take_dve, (t + 1) * CHUNKS)
                dve.wait_ge(s_take_act, (t + 1) * CHUNKS)
                if t >= 1:
                    dve.wait_ge(s_pick_act, t * 2)
                for rows in (slice(0, K_ROWS), slice(K_ROWS, SLOTS)):
                    nc.vector.transpose(blocks[:, rows, 0:MATMULS], inter[:, rows, :]).then_inc(s_blk, 1)
                dve.wait_ge(s_blk, 2 * t + 2)
                nc.vector.tensor_copy(blocks[:, SLOTS - HALF:SLOTS, SLOTS:SLOTS + HALF],
                                      blocks[:, SLOTS - HALF:SLOTS, 0:HALF]).then_inc(s_wrap, 1)
                dve.wait_ge(s_wrap, t + 1)
                nc.vector.tensor_copy(picked(2), partners(2)).then_inc(s_pick_dve, 1)
                fill(t, AFTER_DENSE)
                dve.wait_ge(s_ptr, t * K_TILES + 3)
                nc.vector.tensor_copy(pairs[0:K_PAIRS, 2, :], pt_bank[2][0:K_PAIRS, 0:P]).then_inc(s_pair_dve, 1)
                dve.wait_ge(s_l1, t * 2 + 2)
                for n in (2, 3):
                    last = nc.vector.tensor_scalar(h1[:, n, :], l1_bank[1][:, (n - 2) * P:(n - 1) * P],
                                                   col_sb[:, B1 + n:B1 + n + 1], 0.0, ALU.add, ALU.max)
                last.then_inc(s_h1_dve, 1)
                fill(t, AFTER_LAYER1)
                dve.wait_ge(s_l2, t * 2 + 2)
                nc.vector.tensor_scalar(h2[:, 1, :], l2_bank[1][:, 0:P], col_sb[:, B2 + 1:B2 + 2], 0.0,
                                        ALU.add, ALU.max).then_inc(s_h2_dve, 1)
                if t + 1 < TILES:
                    for g in range(0, NG, 2):
                        if g not in FILL[t]:
                            pack_group(t + 1, g)

        @block.scalar
        def _(act):
            def pack_group(t, g):
                act.wait_ge(s_tr, t * NG + g + 1)
                if t >= 2:
                    act.wait_ge(s_prod, (t - 1) * CHUNKS)
                nc.scalar.copy(*pack(t, g)).then_inc(s_pack[g], 1)

            def fill(t, place):
                if t + 1 < TILES and place < len(FILL[t]):
                    pack_group(t + 1, FILL[t][place])

            def pack_known(t):
                if t >= 2:
                    act.wait_ge(s_prod, (t - 1) * CHUNKS)
                nc.scalar.copy(slots(t, 0, 1 + RESIDENT),
                               known[:, :, t * P:(t + 1) * P].rearrange("d f (q j) -> d q j f", q=QUADS)
                               ).then_inc(s_pack_known, 1)

            def keep(n):
                r, samples = LOOKUPS[n]
                act.wait_ge(s_look, n + 1)
                nc.scalar.copy(known[:, 1 + r, samples],
                               look_bank[n % 2][:, 0:samples.stop - samples.start]).then_inc(s_known, 1)

            act.dma_start(ids_i[:, 0, :], resident_ids[0].partition_broadcast(part_rows)).then_inc(s_idb[0], 16)
            act.dma_start(col_sb[:], columns).then_inc(s_col, 16)
            act.wait_ge(s_first, 1)
            nc.scalar.activation(first[0:1, 1:2], first[0:1, 0:1], ACT.Relu)
            for r in range(RESIDENT):
                act.wait_ge(s_idb[r], 16)
                if r >= 2:
                    act.wait_ge(s_mask, (r - 1) * ROWS_PER_PART)
                nc.scalar.copy(ids_h[:, r % 2, :], ids_i[:, r, :]).then_inc(s_idh, 1)
                if r >= 2:
                    keep(r - 2)
            keep(RESIDENT - 2)
            for g in range(1, NG, 2):
                pack_group(0, g)
            keep(RESIDENT - 1)
            act.wait_ge(s_known, RESIDENT)
            act.wait_ge(s_dense, 16)
            pack_known(0)

            for t in range(TILES):
                if t >= 1:
                    act.wait_ge(s_blk, 2 * t)
                for c in range(CHUNKS):
                    act.wait_ge(s_prod, t * CHUNKS + c + 1)
                    for q in (2, 3):
                        last = nc.scalar.copy(*take(c, q))
                    last.then_inc(s_take_act, 1)
                for k in (0, 1):
                    if k == 0:
                        act.wait_ge(s_blk, 2 * t + 1)
                    else:
                        act.wait_ge(s_wrap, t + 1)
                    nc.scalar.copy(picked(k), partners(k)).then_inc(s_pick_act, 1)
                    act.wait_ge(s_ptr, t * K_TILES + k + 1)
                    nc.scalar.copy(pairs[0:K_PAIRS, k, :], pt_bank[k][0:K_PAIRS, 0:P]).then_inc(s_pair_act, 1)
                fill(t, AFTER_PAIRS)
                act.wait_ge(s_l1, t * 2 + 1)
                for n in (0, 1):
                    last = nc.scalar.activation(h1[:, n, :], l1_bank[0][:, n * P:(n + 1) * P], ACT.Relu,
                                                bias=col_sb[:, B1 + n:B1 + n + 1])
                last.then_inc(s_h1_act, 1)
                if t + 2 < TILES:
                    pack_known(t + 1)
                act.wait_ge(s_l2, t * 2 + 1)
                nc.scalar.activation(h2[:, 0, :], l2_bank[0][:, 0:P], ACT.Relu,
                                     bias=col_sb[:, B2:B2 + 1]).then_inc(s_h2_act, 1)
                fill(t, AFTER_LAYER2)
                act.wait_ge(s_l3, t + 1)
                nc.scalar.copy(y_row[0:1, t * P:(t + 1) * P], y_bank[0:1, 0:P]).then_inc(s_y, 1)
                if t + 1 < TILES:
                    for g in range(1, NG, 2):
                        if g not in FILL[t]:
                            pack_group(t + 1, g)
                        if t + 2 == TILES and g == 1:
                            keep(LATE_AFTER[1])
                            keep(LATE_AFTER[2])
                        if t + 2 == TILES and g == 3:
                            keep(LATE_AFTER[3])
                            act.wait_ge(s_known, len(LOOKUPS))
                            pack_known(t + 1)


def kernel(**inputs):
    import concourse.bacc as bacc
    from concourse.bass_utils import run_bass_kernel_spmd

    tables = [np.asarray(inputs[f"tbl_{f}"]) for f in range(TABLES)]
    by_size = sorted(range(TABLES), key=lambda f: tables[f].shape[0])
    small = sorted(by_size[:RESIDENT])
    large = sorted(by_size[RESIDENT:])
    feature = [0] + [f + 1 for f in small + large]

    row_of = {}
    for a in range(SLOTS):
        for b in range(a + 1, SLOTS):
            row_of[a, b] = D + len(row_of)
    order = []
    for g in range(SLOTS):
        for k in range(1, HALF + 1):
            a, b = feature[g], feature[(g + k) % SLOTS]
            order.append(row_of[min(a, b), max(a, b)])

    w1 = np.asarray(inputs["W_top1"])
    last = w1.shape[0] - D
    ids = np.asarray(inputs["ids"])
    columns = [np.asarray(inputs[name]).reshape(-1, P).T for name in ("b_top1", "b_top2", "W_top3")]
    row_id = np.arange(P * ROWS_PER_PART, dtype=np.float32).reshape(P, ROWS_PER_PART)
    arrays = {
        "dense_t": np.asarray(inputs["r_dense_features"]).T,
        "ids": ids[:, large],
        "resident_ids": ids[:, small].T,
        **{f"tbl_{f}": tables[f] for f in range(TABLES)},
        "w1_pairs": w1[order],
        "w1_dense": np.concatenate([w1[:D], w1[last:]]),
        "w2": inputs["W_top2"],
        "columns": np.concatenate(columns + [row_id], axis=1),
    }
    nc = bacc.Bacc("TRN2", target_bir_lowering=False, num_devices=1)
    sent, aps = {}, {}
    for name, a in arrays.items():
        a = np.ascontiguousarray(a)
        sent[f"in_{name}"] = a
        aps[name] = nc.dram_tensor(f"in_{name}", a.shape, mybir.dt.from_np(a.dtype), kind="ExternalInput").ap()
    out = nc.dram_tensor("out_y", (BATCH, 1), F32, kind="ExternalOutput").ap()
    build(nc, aps["dense_t"], aps["ids"], aps["resident_ids"], [aps[f"tbl_{f}"] for f in small],
          [aps[f"tbl_{f}"] for f in large], aps["w1_pairs"], aps["w1_dense"], aps["w2"], aps["columns"], out)
    r = run_bass_kernel_spmd(nc, [sent], core_ids=[0])
    return r.results[0]["out_y"]
```

```python
from contextlib import ExitStack

import numpy as np

import concourse.bass as bass
from concourse import mybir

F32 = mybir.dt.float32
F16 = mybir.dt.float16
BF16 = mybir.dt.bfloat16
I32 = mybir.dt.int32
ALU = mybir.AluOpType
ACT = mybir.ActivationFunctionType

P = 128
BATCH = 512
D = 128
TABLES = 26
SLOTS = TABLES + 1
SLOT_PITCH = 32
HID1, HID2 = 512, 256
TILES = BATCH // P

RESIDENT = 7
GATHERED = TABLES - RESIDENT
GROUP = 4
LOAD_GROUPS = [range(f, min(f + GROUP, GATHERED)) for f in range(0, GATHERED, GROUP)]
NG = len(LOAD_GROUPS)
ROWS_PER_PART = 8
MAX_RESIDENT_ROWS = 2048
KEPT = 4

QUADS = 4
MATMULS = P // QUADS

HALF = (SLOTS - 1) // 2
ROW_PITCH = 40
K_ROWS = 9
K_PAIRS = K_ROWS * HALF
K_TILES = SLOTS // K_ROWS

AMONG_PRODUCTS, AFTER_PAIRS, AFTER_LAYER1, AFTER_LAYER2 = range(4)
BETWEEN = [8, 17, 25]
FILL = [[[0], [1], [2], [3, 4]]] * (TILES - 2) + [[[], [0, 1], [2], []]]

LOOKUPS = [(0, 0, 4, 1), (1, 0, 4, 0), (2, 0, 4, 1), (3, 0, 3, 0), (4, 0, 3, 1), (5, 0, 2, 0), (6, 0, 2, 1),
           (5, 2, 3, 2), (6, 2, 3, 1), (3, 3, 4, 2), (4, 3, 4, 1), (5, 3, 4, 2), (6, 3, 4, 1)]
EARLY_GROUPS = {4: [0, 1, 2, 3], 5: [4]}
AFTER_PRODUCTS = {0: 7, 1: 9, 2: 11}
AT_END = {0: 8, 1: 10}
STRAIGHT = {0: RESIDENT - 1, TILES - 1: len(LOOKUPS) - 1}

WARM_UP = 9

B1, B2, W3, ROW_ID = 0, HID1 // P, HID1 // P + HID2 // P, HID1 // P + 2 * (HID2 // P)
N_COLS = ROW_ID + ROWS_PER_PART


def build(nc, dense_t, ids, resident_ids, resident, gathered, w1_pairs, w1_dense, w2, columns, out):
    part_rows = resident[0].shape[0] // ROWS_PER_PART
    assert all(t.shape[0] == part_rows * ROWS_PER_PART <= MAX_RESIDENT_ROWS for t in resident)
    assert part_rows <= P

    with ExitStack() as ctx:
        def sb(name, shape, dt=F32):
            return ctx.enter_context(nc.sbuf_tensor(name, shape, dt))

        def sem(name):
            return ctx.enter_context(nc.semaphore(name))

        ids_sb = sb("ids_sb", [P, TILES, GATHERED], I32)
        emb = sb("emb", [P, 2, GATHERED, D])
        ident = sb("ident", [P, P])
        table = sb("table", [part_rows, RESIDENT, ROWS_PER_PART * D])
        rest = sb("rest", [part_rows, KEPT, ROWS_PER_PART * D])
        low = sb("low", [part_rows, KEPT, ROWS_PER_PART, D], BF16)
        ids_i = sb("ids_i", [part_rows, RESIDENT, BATCH], I32)
        ids_h = sb("ids_h", [part_rows, 2, BATCH], F16)
        mask = sb("mask", [part_rows, KEPT, ROWS_PER_PART, BATCH], BF16)
        known = sb("known", [D, 1 + RESIDENT, BATCH])
        xT = sb("xT", [D, 2, MATMULS, QUADS, SLOT_PITCH])
        inter_s = sb("inter_s", [P, SLOTS * (ROW_PITCH + 1) + 1])
        pairs_s = sb("pairs_s", [P, K_TILES, K_PAIRS])
        pairs = sb("pairs", [P, K_TILES, P])
        w1p_sb = sb("w1p_sb", [P, K_TILES, HID1])
        w1d_sb = sb("w1d_sb", [P, 2, HID1])
        w1_sum = sb("w1_sum", [P, HID1])
        w2_sb = sb("w2_sb", [P, HID1 // P, HID2])
        col_sb = sb("col_sb", [P, N_COLS])
        h1 = sb("h1", [P, HID1 // P, P])
        h2 = sb("h2", [P, HID2 // P, P])
        first = sb("first", [1, 2])
        y_row = sb("y_row", [1, BATCH])

        prod = ctx.enter_context(nc.psum_tensor("prod", [P, MATMULS, SLOT_PITCH], F32))
        half_bank = [prod[:, h * MATMULS // 2:(h + 1) * MATMULS // 2, :].rearrange("p j g -> p (j g)")
                     for h in range(2)]
        bank = [ctx.enter_context(nc.psum_tensor(f"bank{i}", [P, 512], F32)) for i in range(6)]
        t_bank = [bank[3], bank[4], bank[5], bank[0], bank[1]]
        pt_bank = [bank[2], half_bank[0], half_bank[1]]
        l1_bank = [bank[0], bank[1]]
        l2_bank = half_bank
        y_bank = bank[2]
        look_bank = [half_bank[0], half_bank[1], t_bank[2]]

        s_ids = sem("s_ids")
        s_idb = [sem(f"s_idb{r}") for r in range(RESIDENT)]
        s_table = [sem(f"s_table{r}") for r in range(RESIDENT)]
        s_dense = sem("s_dense")
        s_w1p = sem("s_w1p")
        s_w1d = sem("s_w1d")
        s_w2 = sem("s_w2")
        s_col = sem("s_col")
        s_gather = [[sem(f"s_gather{b}_{g}") for g in range(NG)] for b in range(2)]
        s_first = sem("s_first")
        s_zero = sem("s_zero")
        s_ident = sem("s_ident")
        s_pad = sem("s_pad")
        s_w1sum = sem("s_w1sum")
        s_idh = sem("s_idh")
        s_mask = sem("s_mask")
        s_rest = sem("s_rest")
        s_low = sem("s_low")
        s_look = sem("s_look")
        s_known = sem("s_known")
        s_tr = sem("s_tr")
        s_pack = [sem(f"s_pack{g}") for g in range(NG)]
        s_pack_end = sem("s_pack_end")
        s_pack_known = sem("s_pack_known")
        s_prod = sem("s_prod")
        s_blk = sem("s_blk")
        s_wrap = sem("s_wrap")
        s_pick_dve = sem("s_pick_dve")
        s_pick_act = sem("s_pick_act")
        s_ptr = sem("s_ptr")
        s_pair_dve = sem("s_pair_dve")
        s_pair_act = sem("s_pair_act")
        s_l1 = sem("s_l1")
        s_h1_act = sem("s_h1_act")
        s_h1_dve = sem("s_h1_dve")
        s_l2 = sem("s_l2")
        s_h2_act = sem("s_h2_act")
        s_h2_dve = sem("s_h2_dve")
        s_l3 = sem("s_l3")
        s_y = sem("s_y")
        s_out = sem("s_out")

        blocks = inter_s[:, 0:SLOTS * ROW_PITCH].rearrange("s (g f) -> s g f", f=ROW_PITCH)

        def upper_halves(words):
            return words.bitcast(BF16).rearrange("p (k d two) -> p k d two", k=ROWS_PER_PART, two=2)[:, :, :, 1]

        def by_row(words):
            return words.rearrange("p (k d) -> p k d", k=ROWS_PER_PART)

        def partners(k):
            first = (ROW_PITCH + 1) * K_ROWS * k + 1
            rows = inter_s[:, first:first + K_ROWS * (ROW_PITCH + 1)]
            return rows.rearrange("s (g f) -> s g f", g=K_ROWS)[:, :, 0:HALF]

        def picked(k):
            return pairs_s[:, k, :].rearrange("s (g f) -> s g f", g=K_ROWS)

        def slots(t, first, n):
            return xT[:, t % 2, :, :, first:first + n].rearrange("d j q f -> d q j f")

        def pack(t, g, half=None):
            n = len(LOAD_GROUPS[g])
            js = slice(0, MATMULS) if half is None else slice(half * MATMULS // 2, (half + 1) * MATMULS // 2)
            return (slots(t, 1 + RESIDENT + LOAD_GROUPS[g].start, n)[:, :, js, :],
                    t_bank[g][:, 0:n * P].rearrange("d (f q j) -> d q j f", f=n, q=QUADS)[:, :, js, :])

        def look_dst(n):
            _, first, end, b = LOOKUPS[n]
            return look_bank[b][:, 0:(end - first) * P]

        def lookups_for(t):
            return max(n + 1 for n, (_, first, end, _) in enumerate(LOOKUPS) if first <= t < end)

        def lookups_before(t):
            return RESIDENT + sum(t > u for u in [*AT_END, *AFTER_PRODUCTS])

        block = ctx.enter_context(nc.Block())

        @block.sync
        def _(sp):
            sp.dma_start(ids_sb[:], ids.rearrange("(t s) f -> s t f", s=P)).then_inc(s_ids, 16)
            for r in range(RESIDENT):
                if r >= 1:
                    sp.dma_start(ids_i[:, r, :], resident_ids[r].partition_broadcast(part_rows)).then_inc(s_idb[r], 16)
                sp.dma_start(table[:, r, :], resident[r].rearrange("(p k) d -> p (k d)", k=ROWS_PER_PART)
                             ).then_inc(s_table[r], 16)
            sp.dma_start(known[:, 0, :], dense_t).then_inc(s_dense, 16)
            sp.dma_start(w1d_sb[:], w1_dense.rearrange("(c p) n -> p c n", p=P)).then_inc(s_w1d, 16)
            sp.dma_start(w1p_sb[0:K_PAIRS], w1_pairs.rearrange("(k p) n -> p k n", p=K_PAIRS)).then_inc(s_w1p, 16)
            sp.dma_start(w2_sb[:], w2.rearrange("(c p) n -> p c n", p=P)).then_inc(s_w2, 16)
            sp.wait_ge(s_y, TILES)
            sp.dma_start(out.rearrange("b o -> o b"), y_row[:]).then_inc(s_out, 16)
            sp.wait_ge(s_out, 16)

        @block.gpsimd
        def _(pool):
            nc.gpsimd.memset(ident[:], 0.0).then_inc(s_zero, 1)
            pool.wait_ge(s_zero, 1)
            nc.gpsimd.affine_select(out=ident[:], in_=ident[:], compare_op=ALU.not_equal, fill=1.0, base=0,
                                    pattern=[[-1, P]], channel_multiplier=1).then_inc(s_ident, 1)
            for b in range(2):
                nc.gpsimd.memset(xT[:, b, :, :, SLOTS:SLOT_PITCH], 0.0).then_inc(s_pad, 1)
            pool.wait_ge(s_ids, 16)
            for t in range(TILES):
                for g in range(NG):
                    if t >= 2:
                        pool.wait_ge(s_tr, NG * (t - 2) + g + 1)
                    for f in LOAD_GROUPS[g]:
                        nc.gpsimd.indirect_dma_start(
                            out=emb[:, t % 2, f, :], out_offset=None, in_=gathered[f],
                            in_offset=bass.IndirectOffsetOnAxis(ap=ids_sb[:, t, f:f + 1], axis=0),
                        ).then_inc(s_gather[t % 2][g], 16)

        @block.tensor
        def _(pe):
            def look_up(n):
                r, first, end, b = LOOKUPS[n]
                samples = slice(first * P, end * P)
                before = [m for m in range(n) if LOOKUPS[m][3] == b]
                if before:
                    pe.wait_ge(s_known, before[-1] + 1)
                pe.wait_ge(s_table[r], 16)
                for part in range(3):
                    if part == 1:
                        pe.wait_ge(s_rest, r + 1)
                    if part == 2:
                        pe.wait_ge(s_low, r + 1)
                    src = [upper_halves(table[:, r, :]), upper_halves(rest[:, r % KEPT, :]), low[:, r % KEPT]][part]
                    for k in range(ROWS_PER_PART):
                        if part == 0:
                            pe.wait_ge(s_mask, r * ROWS_PER_PART + k + 1)
                        mm = nc.tensor.matmul(look_dst(n), src[:, k, :], mask[:, r % KEPT, k, samples],
                                              start=(part == 0 and k == 0),
                                              stop=(part == 2 and k == ROWS_PER_PART - 1))
                mm.then_inc(s_look, 1)

            def turn(t, g):
                if t >= 1 and g in (3, 4):
                    pe.wait_ge((s_h1_act, s_h1_dve)[g - 3], t)
                if t >= 1 and g == 2:
                    pe.wait_ge(s_known, AFTER_PRODUCTS[t - 1] + 1)
                pe.wait_ge(s_gather[t % 2][g], (t // 2 + 1) * 16 * len(LOAD_GROUPS[g]))
                for i, f in enumerate(LOAD_GROUPS[g]):
                    mm = nc.tensor.transpose(t_bank[g][:, i * P:(i + 1) * P],
                                             emb[:, t % 2, f, :], ident[:])
                mm.then_inc(s_tr, 1)

            def fill(t, place):
                for g in FILL[t][place] if t + 1 < TILES else ():
                    turn(t + 1, g)

            def layer1(n, weights, x, last):
                return nc.tensor.matmul(l1_bank[n // 2][:, (n % 2) * P:(n % 2 + 1) * P],
                                        weights[:, n * P:(n + 1) * P], x,
                                        start=(weights is w1_sum and n % 2 == 0), stop=last,
                                        skip_group_check=True)

            def between(t, place):
                if place == 1:
                    fill(t, AMONG_PRODUCTS)
                pe.wait_ge(s_w1sum, 1)
                for n in range(HID1 // P):
                    if n // 2 == place // 2 and place != 1:
                        layer1(n, w1_sum, known[:, 0, t * P:(t + 1) * P], False)

            def interact(t):
                pe.wait_ge(s_pad, 2)
                pe.wait_ge(s_pack_known, t + 1 + sum(u <= t for u in STRAIGHT))
                for g in range(NG):
                    pe.wait_ge(s_pack[g], t + 1)
                for i in range(MATMULS):
                    if i == MATMULS // 2:
                        pe.wait_ge(s_pack_end, t + 1)
                        pe.wait_ge(s_known, lookups_before(t))
                    if i in BETWEEN:
                        between(t, BETWEEN.index(i))
                    for q in range(QUADS):
                        x = xT[:, t % 2, i, q, :]
                        mm = nc.tensor.matmul(prod[SLOT_PITCH * q:SLOT_PITCH * (q + 1), i, :], x, x,
                                              start=True, stop=True)
                mm.then_inc(s_prod, 1)

            def mlp(t):
                pe.wait_ge(s_w1p, 16)
                if t in AFTER_PRODUCTS:
                    look_up(AFTER_PRODUCTS[t])
                for k in range(K_TILES):
                    if k == K_TILES - 1:
                        pe.wait_ge(s_pick_dve, t + 1)
                    else:
                        pe.wait_ge(s_pick_act, t * 2 + k + 1)
                    if k == 0 and t >= 1:
                        pe.wait_ge(s_y, t)
                    nc.tensor.transpose(pt_bank[k][0:K_PAIRS, 0:P], pairs_s[:, k, :], ident[:]).then_inc(s_ptr, 1)
                    if k == 0:
                        fill(t, AFTER_PAIRS)
                pe.wait_ge(s_pair_act, t * 2 + 1)
                for n in range(HID1 // P):
                    layer1(n, w1p_sb[0:K_PAIRS, 0, :], pairs[0:K_PAIRS, 0, :], False)
                for n in range(HID1 // P):
                    for k in range(1, K_TILES):
                        if n == 0 and k == 1:
                            pe.wait_ge(s_pair_act, t * 2 + 2)
                        elif n == 0:
                            pe.wait_ge(s_pair_dve, t + 1)
                        mm = layer1(n, w1p_sb[0:K_PAIRS, k, :], pairs[0:K_PAIRS, k, :], k == K_TILES - 1)
                    if n % 2:
                        mm.then_inc(s_l1, 1)
                fill(t, AFTER_LAYER1)
                pe.wait_ge(s_w2, 16)
                for half in range(2):
                    pe.wait_ge((s_h1_act, s_h1_dve)[half], t + 1)
                    for m in range(HID2 // P):
                        for c in (2 * half, 2 * half + 1):
                            mm = nc.tensor.matmul(l2_bank[m][:, 0:P], w2_sb[:, c, m * P:(m + 1) * P], h1[:, c, :],
                                                  start=(c == 0), stop=(c == HID1 // P - 1))
                        if half == 1:
                            mm.then_inc(s_l2, 1)
                fill(t, AFTER_LAYER2)
                for m in range(HID2 // P):
                    pe.wait_ge((s_h2_act, s_h2_dve)[m], t + 1)
                    mm = nc.tensor.matmul(y_bank[0:1, 0:P], col_sb[:, W3 + m:W3 + m + 1], h2[:, m, :],
                                          start=(m == 0), stop=(m == HID2 // P - 1))
                mm.then_inc(s_l3, 1)

            pe.wait_ge(s_ident, 1)
            for _ in range(WARM_UP):
                nc.tensor.matmul(half_bank[1][:, 0:P], ident[:], ident[:], start=True, stop=True)
            for r in range(RESIDENT):
                look_up(r)
                for g in EARLY_GROUPS.get(r, ()):
                    turn(0, g)
            for t in range(TILES):
                interact(t)
                mlp(t)
                if t + 2 == TILES:
                    for g in range(3, NG):
                        turn(t + 1, g)
                    look_up(STRAIGHT[t + 1])
                elif t + 1 < TILES:
                    look_up(AT_END[t])

        @block.vector
        def _(dve):
            def pack_group(t, g):
                dve.wait_ge(s_tr, t * NG + g + 1)
                if t >= 2:
                    dve.wait_ge(s_prod, t - 1)
                if g < NG - 1:
                    nc.vector.tensor_copy(*pack(t, g)).then_inc(s_pack[g], 1)
                else:
                    nc.vector.tensor_copy(*pack(t, g, 0)).then_inc(s_pack[g], 1)
                    nc.vector.tensor_copy(*pack(t, g, 1)).then_inc(s_pack_end, 1)

            def fill(t, place):
                for g in FILL[t][place] if t + 1 < TILES else ():
                    if g % 2 == 0:
                        pack_group(t + 1, g)

            nc.vector.memset(first[:], 0.0).then_inc(s_first, 1)
            dve.wait_ge(s_col, 16)
            for r in range(RESIDENT):
                dve.wait_ge(s_idh, r + 1)
                if r >= KEPT:
                    dve.wait_ge(s_look, r - KEPT + 1)
                for k in range(ROWS_PER_PART):
                    nc.vector.tensor_scalar(mask[:, r % KEPT, k, :], ids_h[:, r % 2, :],
                                            col_sb[0:part_rows, ROW_ID + k:ROW_ID + k + 1], None,
                                            ALU.is_equal).then_inc(s_mask, 1)
                dve.wait_ge(s_table[r], 16)
                nc.vector.tensor_tensor(by_row(rest[:, r % KEPT, :]), by_row(table[:, r, :]),
                                        upper_halves(table[:, r, :]), ALU.subtract).then_inc(s_rest, 1)
                dve.wait_ge(s_rest, r + 1)
                nc.vector.tensor_tensor(low[:, r % KEPT], by_row(rest[:, r % KEPT, :]),
                                        upper_halves(rest[:, r % KEPT, :]), ALU.subtract).then_inc(s_low, 1)
            dve.wait_ge(s_w1d, 16)
            nc.vector.tensor_tensor(w1_sum[:], w1d_sb[:, 0, :], w1d_sb[:, 1, :], ALU.add).then_inc(s_w1sum, 1)

            for t in range(TILES):
                fill(t, AMONG_PRODUCTS)
                dve.wait_ge(s_prod, t + 1)
                if t >= 1:
                    dve.wait_ge(s_pick_act, t * 2)
                for rows in (slice(0, K_ROWS), slice(K_ROWS, SLOTS)):
                    nc.vector.transpose(blocks[:, rows, 0:MATMULS],
                                        prod[:, :, rows].rearrange("p j g -> p g j")).then_inc(s_blk, 1)
                dve.wait_ge(s_blk, 2 * t + 2)
                nc.vector.tensor_copy(blocks[:, SLOTS - HALF:SLOTS, SLOTS:SLOTS + HALF],
                                      blocks[:, SLOTS - HALF:SLOTS, 0:HALF]).then_inc(s_wrap, 1)
                dve.wait_ge(s_wrap, t + 1)
                nc.vector.tensor_copy(picked(2), partners(2)).then_inc(s_pick_dve, 1)
                dve.wait_ge(s_ptr, t * K_TILES + 3)
                nc.vector.tensor_copy(pairs[0:K_PAIRS, 2, :], pt_bank[2][0:K_PAIRS, 0:P]).then_inc(s_pair_dve, 1)
                fill(t, AFTER_PAIRS)
                dve.wait_ge(s_l1, t * 2 + 2)
                for n in (2, 3):
                    last = nc.vector.tensor_scalar(h1[:, n, :], l1_bank[1][:, (n - 2) * P:(n - 1) * P],
                                                   col_sb[:, B1 + n:B1 + n + 1], 0.0, ALU.add, ALU.max)
                last.then_inc(s_h1_dve, 1)
                fill(t, AFTER_LAYER1)
                dve.wait_ge(s_l2, t * 2 + 2)
                nc.vector.tensor_scalar(h2[:, 1, :], l2_bank[1][:, 0:P], col_sb[:, B2 + 1:B2 + 2], 0.0,
                                        ALU.add, ALU.max).then_inc(s_h2_dve, 1)
                fill(t, AFTER_LAYER2)
                if t + 2 == TILES:
                    pack_group(t + 1, NG - 1)

        @block.scalar
        def _(act):
            def pack_group(t, g):
                act.wait_ge(s_tr, t * NG + g + 1)
                if t >= 2:
                    act.wait_ge(s_prod, t - 1)
                nc.scalar.copy(*pack(t, g)).then_inc(s_pack[g], 1)

            def fill(t, place):
                for g in FILL[t][place] if t + 1 < TILES else ():
                    if g % 2 == 1:
                        pack_group(t + 1, g)

            def pack_known(t, n):
                act.wait_ge(s_known, lookups_for(t) - (t in STRAIGHT))
                if t >= 2:
                    act.wait_ge(s_prod, t - 1)
                nc.scalar.copy(slots(t, 0, n),
                               known[:, 0:n, t * P:(t + 1) * P].rearrange("d f (q j) -> d q j f", q=QUADS)
                               ).then_inc(s_pack_known, 1)

            def pack_straight(t):
                act.wait_ge(s_look, STRAIGHT[t] + 1)
                nc.scalar.copy(slots(t, RESIDENT, 1), look_dst(STRAIGHT[t])[:, 0:P].rearrange(
                    "d (f q j) -> d q j f", f=1, q=QUADS)).then_inc(s_pack_known, 1)

            def keep(n):
                r, first, end, _ = LOOKUPS[n]
                act.wait_ge(s_look, n + 1)
                nc.scalar.copy(known[:, 1 + r, first * P:end * P], look_dst(n)).then_inc(s_known, 1)

            act.dma_start(ids_i[:, 0, :], resident_ids[0].partition_broadcast(part_rows)).then_inc(s_idb[0], 16)
            act.dma_start(col_sb[:], columns).then_inc(s_col, 16)
            act.wait_ge(s_first, 1)
            nc.scalar.activation(first[0:1, 1:2], first[0:1, 0:1], ACT.Relu)
            for r in range(RESIDENT):
                act.wait_ge(s_idb[r], 16)
                if r >= 2:
                    act.wait_ge(s_mask, (r - 1) * ROWS_PER_PART)
                nc.scalar.copy(ids_h[:, r % 2, :], ids_i[:, r, :]).then_inc(s_idh, 1)
                if r >= 2:
                    keep(r - 2)
            for r in sorted(EARLY_GROUPS):
                for g in EARLY_GROUPS[r]:
                    act.wait_ge(s_tr, g + 1)
                    nc.scalar.copy(*pack(0, g, 0 if g == NG - 1 else None)).then_inc(s_pack[g], 1)
                    if g == NG - 1:
                        nc.scalar.copy(*pack(0, g, 1)).then_inc(s_pack_end, 1)
                if r == RESIDENT - 3:
                    keep(RESIDENT - 2)
            act.wait_ge(s_dense, 16)
            pack_known(0, RESIDENT)
            pack_straight(0)
            keep(RESIDENT - 1)

            for t in range(TILES):
                for k in (0, 1):
                    if k == 0:
                        act.wait_ge(s_blk, 2 * t + 1)
                    else:
                        act.wait_ge(s_wrap, t + 1)
                    nc.scalar.copy(picked(k), partners(k)).then_inc(s_pick_act, 1)
                    act.wait_ge(s_ptr, t * K_TILES + k + 1)
                    nc.scalar.copy(pairs[0:K_PAIRS, k, :], pt_bank[k][0:K_PAIRS, 0:P]).then_inc(s_pair_act, 1)
                fill(t, AFTER_PAIRS)
                if t in AFTER_PRODUCTS:
                    keep(AFTER_PRODUCTS[t])
                act.wait_ge(s_l1, t * 2 + 1)
                for n in (0, 1):
                    last = nc.scalar.activation(h1[:, n, :], l1_bank[0][:, n * P:(n + 1) * P], ACT.Relu,
                                                bias=col_sb[:, B1 + n:B1 + n + 1])
                last.then_inc(s_h1_act, 1)
                if t + 2 < TILES:
                    pack_known(t + 1, 1 + RESIDENT)
                act.wait_ge(s_l2, t * 2 + 1)
                nc.scalar.activation(h2[:, 0, :], l2_bank[0][:, 0:P], ACT.Relu,
                                     bias=col_sb[:, B2:B2 + 1]).then_inc(s_h2_act, 1)
                fill(t, AFTER_LAYER2)
                act.wait_ge(s_l3, t + 1)
                nc.scalar.copy(y_row[0:1, t * P:(t + 1) * P], y_bank[0:1, 0:P]).then_inc(s_y, 1)
                if t + 2 == TILES:
                    pack_known(t + 1, RESIDENT)
                    pack_group(t + 1, 3)
                    pack_straight(t + 1)
                elif t + 1 < TILES:
                    keep(AT_END[t])


def kernel(**inputs):
    import concourse.bacc as bacc
    from concourse.bass_utils import run_bass_kernel_spmd

    tables = [np.asarray(inputs[f"tbl_{f}"]) for f in range(TABLES)]
    by_size = sorted(range(TABLES), key=lambda f: tables[f].shape[0])
    small = sorted(by_size[:RESIDENT])
    large = sorted(by_size[RESIDENT:])
    feature = [0] + [f + 1 for f in small + large]

    row_of = {}
    for a in range(SLOTS):
        for b in range(a + 1, SLOTS):
            row_of[a, b] = D + len(row_of)
    order = []
    for g in range(SLOTS):
        for k in range(1, HALF + 1):
            a, b = feature[g], feature[(g + k) % SLOTS]
            order.append(row_of[min(a, b), max(a, b)])

    w1 = np.asarray(inputs["W_top1"])
    last = w1.shape[0] - D
    ids = np.asarray(inputs["ids"])
    columns = [np.asarray(inputs[name]).reshape(-1, P).T for name in ("b_top1", "b_top2", "W_top3")]
    row_id = np.arange(P * ROWS_PER_PART, dtype=np.float32).reshape(P, ROWS_PER_PART)
    arrays = {
        "dense_t": np.asarray(inputs["r_dense_features"]).T,
        "ids": ids[:, large],
        "resident_ids": ids[:, small].T,
        **{f"tbl_{f}": tables[f] for f in range(TABLES)},
        "w1_pairs": w1[order],
        "w1_dense": np.concatenate([w1[:D], w1[last:]]),
        "w2": inputs["W_top2"],
        "columns": np.concatenate(columns + [row_id], axis=1),
    }
    nc = bacc.Bacc("TRN2", target_bir_lowering=False, num_devices=1)
    sent, aps = {}, {}
    for name, a in arrays.items():
        a = np.ascontiguousarray(a)
        sent[f"in_{name}"] = a
        aps[name] = nc.dram_tensor(f"in_{name}", a.shape, mybir.dt.from_np(a.dtype), kind="ExternalInput").ap()
    out = nc.dram_tensor("out_y", (BATCH, 1), F32, kind="ExternalOutput").ap()
    build(nc, aps["dense_t"], aps["ids"], aps["resident_ids"], [aps[f"tbl_{f}"] for f in small],
          [aps[f"tbl_{f}"] for f in large], aps["w1_pairs"], aps["w1_dense"], aps["w2"], aps["columns"], out)
    r = run_bass_kernel_spmd(nc, [sent], core_ids=[0])
    return r.results[0]["out_y"]
```
